# Optimizing a Trainium2 kernel written in Bass

```python
import numpy as np
import jax
import jax.numpy as jnp

def _softmax(x, axis=-1):
    return jax.nn.softmax(x, axis=axis)
def _gelu(x):
    return jax.nn.gelu(x, approximate=True)
def _silu(x):
    return jax.nn.silu(x)
def _sigmoid(x):
    return jax.nn.sigmoid(x)
def _layernorm(x, axis=-1, eps=1e-5):
    m = jnp.mean(x, axis=axis, keepdims=True)
    v = jnp.var(x, axis=axis, keepdims=True)
    return (x - m) / jnp.sqrt(v + eps)
def _scatter_add(tgt, idx, src, axis=0):
    return tgt.at[idx].add(src)
def _segment_sum(src, seg, n):
    return jax.ops.segment_sum(src, seg, n)

kernel_name = 'mk_conv_preact_d2_conv_nchw384_8fb925'

def setup_inputs(seed: int = 0):
    np.random.seed(seed)
    _w = jnp.asarray
    def _rec_inputs():
        import jax
        import jax.numpy as jnp
        _gk = jax.random.key(seed)
        x = -4.65e-05 + 0.9999 * jax.random.normal(jax.random.fold_in(_gk, 1), (32, 384, 64, 64), jnp.float32)
        return x
    x = _rec_inputs()
    def _L0_conv_setup():
        import jax, jax.numpy as jnp
        import numpy as np
        H, W = (64, 64)
        STRIDE = 16
        NUM_Y = (H - STRIDE) // STRIDE * 2 + 1
        NUM_X = (W - STRIDE) // STRIDE * 2 + 1
        NUM_POS = NUM_Y * NUM_X - 1
        CHAN_PER_POS = 8
        C = NUM_POS * CHAN_PER_POS
        B = 32
        K = 3
        SIGMA = 0.5

        def _init_offset():
            offs = []
            for ih in range(-(NUM_Y // 2), NUM_Y // 2 + 1):
                for iw in range(-(NUM_X // 2), NUM_X // 2 + 1):
                    if ih == 0 and iw == 0:
                        continue
                    offs.append([iw * STRIDE, ih * STRIDE])
            return np.asarray(offs, dtype=np.float32)

        def _displace(x, off_int):
            xg = x.reshape(B, NUM_POS, CHAN_PER_POS, H, W)
            ox, oy = (off_int[:, 0], off_int[:, 1])
            ys = jnp.arange(H)[None, :] - oy[:, None]
            xs = jnp.arange(W)[None, :] - ox[:, None]
            vy = (ys >= 0) & (ys < H)
            vx = (xs >= 0) & (xs < W)
            ysc = jnp.clip(ys, 0, H - 1)
            xsc = jnp.clip(xs, 0, W - 1)
            g = jnp.take_along_axis(xg, ysc[None, :, None, :, None], axis=3)
            g = jnp.take_along_axis(g, xsc[None, :, None, None, :], axis=4)
            mask = (vy[:, :, None] & vx[:, None, :])[None, :, None, :, :]
            return jnp.where(mask, g, 0.0).reshape(B, C, H, W)
        key = jax.random.key(seed)
        k1, k2 = jax.random.split(key)
        inp = jax.random.normal(k1, (B, C, H, W), dtype=jnp.float32)
        offset = jnp.asarray(_init_offset()) + jax.random.uniform(k2, (NUM_POS, 2), minval=-0.45, maxval=0.45, dtype=jnp.float32)
        return {'inp': inp, 'offset': offset}
    _L0_conv_all = _L0_conv_setup()
    _L0_conv_in = {k: v for k, v in _L0_conv_all.items() if k in ('offset', )}
    del _L0_conv_all

    def _L1_conv_setup():
        import jax, jax.numpy as jnp
        import numpy as np
        C = 384

        def dwconv(x, w, pad_h, pad_w, stride=(1, 1)):
            return jax.lax.conv_general_dilated(x, w, window_strides=stride, padding=((pad_h, pad_h), (pad_w, pad_w)), dimension_numbers=('NCHW', 'OIHW', 'NCHW'), feature_group_count=C)
        key = jax.random.key(seed)
        ks = jax.random.split(key, 12)
        f = lambda k, shape: jax.random.normal(k, shape, dtype=jnp.float32) * 0.05
        return {'x': jax.random.normal(ks[0], (32, C, 56, 56), dtype=jnp.float32), 'w77': f(ks[1], (C, 1, 7, 7)), 'b77': f(ks[2], (C,)), 'w53': f(ks[3], (C, 1, 5, 3)), 'b53': f(ks[4], (C,)), 'w35': f(ks[5], (C, 1, 3, 5)), 'b35': f(ks[6], (C,)), 'w7w': f(ks[7], (C, 1, 1, 7)), 'w7h': f(ks[8], (C, 1, 7, 1)), 'w5w': f(ks[9], (C, 1, 1, 5)), 'w5h': f(ks[10], (C, 1, 5, 1))}
    _L1_conv_all = _L1_conv_setup()
    _L1_conv_in = {k: v for k, v in _L1_conv_all.items() if k in ('w77', 'b77', 'w53', 'b53', 'w35', 'b35', 'w7w', 'w7h', 'w5w', 'w5h', )}
    del _L1_conv_all

    return {
        "x": x,
        "L0_conv_offset": _L0_conv_in["offset"],
        "L1_conv_w77": _L1_conv_in["w77"],
        "L1_conv_b77": _L1_conv_in["b77"],
        "L1_conv_w53": _L1_conv_in["w53"],
        "L1_conv_b53": _L1_conv_in["b53"],
        "L1_conv_w35": _L1_conv_in["w35"],
        "L1_conv_b35": _L1_conv_in["b35"],
        "L1_conv_w7w": _L1_conv_in["w7w"],
        "L1_conv_w7h": _L1_conv_in["w7h"],
        "L1_conv_w5w": _L1_conv_in["w5w"],
        "L1_conv_w5h": _L1_conv_in["w5h"],
    }

def reference(x, L0_conv_offset, L1_conv_w77, L1_conv_b77, L1_conv_w53, L1_conv_b53, L1_conv_w35, L1_conv_b35, L1_conv_w7w, L1_conv_w7h, L1_conv_w5w, L1_conv_w5h):
    import jax
    import jax.numpy as jnp
    def _L0_conv_ref(inp, offset):
        import jax, jax.numpy as jnp
        import numpy as np
        H, W = (64, 64)
        STRIDE = 16
        NUM_Y = (H - STRIDE) // STRIDE * 2 + 1
        NUM_X = (W - STRIDE) // STRIDE * 2 + 1
        NUM_POS = NUM_Y * NUM_X - 1
        CHAN_PER_POS = 8
        C = NUM_POS * CHAN_PER_POS
        B = 32
        K = 3
        SIGMA = 0.5

        def _init_offset():
            offs = []
            for ih in range(-(NUM_Y // 2), NUM_Y // 2 + 1):
                for iw in range(-(NUM_X // 2), NUM_X // 2 + 1):
                    if ih == 0 and iw == 0:
                        continue
                    offs.append([iw * STRIDE, ih * STRIDE])
            return np.asarray(offs, dtype=np.float32)

        def _displace(x, off_int):
            xg = x.reshape(B, NUM_POS, CHAN_PER_POS, H, W)
            ox, oy = (off_int[:, 0], off_int[:, 1])
            ys = jnp.arange(H)[None, :] - oy[:, None]
            xs = jnp.arange(W)[None, :] - ox[:, None]
            vy = (ys >= 0) & (ys < H)
            vx = (xs >= 0) & (xs < W)
            ysc = jnp.clip(ys, 0, H - 1)
            xsc = jnp.clip(xs, 0, W - 1)
            g = jnp.take_along_axis(xg, ysc[None, :, None, :, None], axis=3)
            g = jnp.take_along_axis(g, xsc[None, :, None, None, :], axis=4)
            mask = (vy[:, :, None] & vx[:, None, :])[None, :, None, :, :]
            return jnp.where(mask, g, 0.0).reshape(B, C, H, W)
        off_round = jax.lax.stop_gradient(jnp.round(offset))
        out = _displace(inp, off_round.astype(jnp.int32))
        frac = offset - off_round
        coords = jnp.arange(K, dtype=jnp.float32) - float(K // 2)
        field_x = jnp.broadcast_to(coords[None, :], (K, K))
        field_y = jnp.broadcast_to(coords[:, None], (K, K))
        dx = field_x[None] + frac[:, None, None, 0]
        dy = field_y[None] + frac[:, None, None, 1]
        kern = jnp.exp(-(dx * dx + dy * dy) / (2.0 * SIGMA ** 2))
        kern = kern / jnp.sum(kern, axis=(1, 2), keepdims=True)
        kern = jnp.repeat(kern[:, None, :, :], CHAN_PER_POS, axis=1)
        kern = kern.reshape(C, 1, K, K)
        out = jax.lax.conv_general_dilated(out, kern, window_strides=(1, 1), padding=[(K // 2, K // 2), (K // 2, K // 2)], dimension_numbers=('NCHW', 'OIHW', 'NCHW'), feature_group_count=C)
        return out

    def _L1_conv_ref(x, w77, b77, w53, b53, w35, b35, w7w, w7h, w5w, w5h):
        import jax, jax.numpy as jnp
        import numpy as np
        C = 384

        def dwconv(x, w, pad_h, pad_w, stride=(1, 1)):
            return jax.lax.conv_general_dilated(x, w, window_strides=stride, padding=((pad_h, pad_h), (pad_w, pad_w)), dimension_numbers=('NCHW', 'OIHW', 'NCHW'), feature_group_count=C)
        bias = (b77 + b53 + b35)[None, :, None, None]
        out = dwconv(x, w77, 3, 3) + dwconv(x, w53, 2, 1) + dwconv(x, w35, 1, 2) + dwconv(dwconv(x, w7w, 0, 3), w7h, 3, 0) + dwconv(dwconv(x, w5w, 0, 2), w5h, 2, 0) + bias
        return out

    def _gn(v, G=32, eps=1e-5):
        B_, C_, H_, W_ = v.shape
        g = v.reshape(B_, G, C_ // G, H_, W_)
        m = jnp.mean(g, axis=(2, 3, 4), keepdims=True)
        s = jnp.var(g, axis=(2, 3, 4), keepdims=True)
        return ((g - m) / jnp.sqrt(s + eps)).reshape(v.shape)

    def _ln_c(v, eps=1e-6):
        m = jnp.mean(v, axis=1, keepdims=True)
        s = jnp.var(v, axis=1, keepdims=True)
        return (v - m) / jnp.sqrt(s + eps)

    def _ln_t(v, eps=1e-5):
        m = jnp.mean(v, axis=-1, keepdims=True)
        s = jnp.var(v, axis=-1, keepdims=True)
        return (v - m) / jnp.sqrt(s + eps)

    def _to_tokens(v):
        B_, C_, H_, W_ = v.shape
        return v.reshape(B_, C_, H_ * W_).transpose(0, 2, 1)
    def _from_tokens(t, like):
        B_, C_, H_, W_ = like.shape
        return t.transpose(0, 2, 1).reshape(B_, C_, H_, W_)

    x = x + _L0_conv_ref(_gn(x), L0_conv_offset)
    x = x + _L1_conv_ref(_gn(x), L1_conv_w77, L1_conv_b77, L1_conv_w53, L1_conv_b53, L1_conv_w35, L1_conv_b35, L1_conv_w7w, L1_conv_w7h, L1_conv_w5w, L1_conv_w5h)
    return x


_drawn_inputs = setup_inputs


def setup_inputs(seed=0):
    import zlib

    import numpy as np

    out = dict(_drawn_inputs(seed))
    spreads = {}
    factors = {'L1_conv_w7w': 3.788, 'L1_conv_w7h': 3.897, 'L1_conv_w5w': 4.946, 'L1_conv_w5h': 5.091}
    for name, (base, spread) in spreads.items():
        noise = np.random.default_rng([zlib.crc32(name.encode()), seed]).standard_normal(out[name].shape)
        drawn = base * np.exp(spread * noise) if base else spread * noise
        out[name] = jnp.asarray(drawn.astype(out[name].dtype))
    for name, factor in factors.items():
        out[name] = (out[name] * factor).astype(out[name].dtype)
    return out
```

```python
import concourse.bass as bass
from concourse import mybir
from contextlib import ExitStack


class Count:

    def __init__(self, g, a, b):
        self.g, self.a, self.b = g, a, b

    def __add__(self, n):
        return Count(self.g, self.a, self.b + n)

    def __sub__(self, n):
        return Count(self.g, self.a, self.b - n)

    def __mul__(self, n):
        return Count(self.g, self.a * n, self.b * n)

    __radd__, __rmul__ = __add__, __mul__

    def address(self):
        return self.g * self.a + self.b


def address(n):
    return n if isinstance(n, int) else n.address()


def conv_block_kernel(nc, x, offset, w77, b77, w53, b53, w35, b35, w7w, w7h, w5w, w5h, out):
    f32, f16, i32 = mybir.dt.float32, mybir.dt.float16, mybir.dt.int32
    ALU, AX = mybir.AluOpType, mybir.AxisListType
    ACT = mybir.ActivationFunctionType
    IDENT, EXP, SQRT = ACT.Identity, ACT.Exp, ACT.Sqrt

    B, C, H, W = x.shape
    P = 128
    GC = 12
    NG = C // GC
    BC = 4
    NQ = GC // BC
    NH = 2
    PERIOD = NH * NQ
    NI = B // NH // 2
    NP = NI * W
    BLK = BC * NP
    NBLOCKS = NG * PERIOD
    DMAS = 16 * BC * 2
    LAG = 4
    UNITS = 3
    PC = 8
    NPOS = C // PC
    K = 7
    R = K // 2
    TAPS = 2 * K
    PITCH = P + K - 1
    ROW = TAPS * PITCH
    FIRST = P - 1 - 2 * R
    ISTR = W + 4
    NPAD = 4 + BC * NI * ISTR + 4
    N0STR = 2 * W
    ACT_SCALE = 64.0
    L0_SCALE = 256.0
    EPS = 1e-5
    KTOP = 128.0
    CP = min(P, C)
    CT = C // CP

    x_v = x.rearrange("(h i r) (g q c) y x -> g q c h r y i x", h=NH, r=2, q=NQ, c=BC)
    out_v = out.rearrange("(h i r) (g q c) y x -> g q c h r y i x", h=NH, r=2, q=NQ, c=BC)

    hankel_d = nc.dram_tensor("hankel_scratch", (C * ROW + P,), f16, kind="Internal").ap()
    shift_d = nc.dram_tensor("shift_scratch", (NPOS, 2, P, 2 * P), f16, kind="Internal").ap()
    l0_coef_d = nc.dram_tensor("l0_coef_scratch", (NPOS, 2, 4), f32, kind="Internal").ap()
    l1_coef_d = nc.dram_tensor("l1_coef_scratch", (C, 4), f32, kind="Internal").ap()
    shift_v = shift_d.rearrange("n d p m -> (n d) p m")
    l0_coef_v = l0_coef_d.rearrange("n d k -> (n d) k")

    ctx = ExitStack()
    with ctx:
        def sb(name, shape, dt):
            return ctx.enter_context(nc.sbuf_tensor(name, shape, dt))

        def pb(name, shape):
            return ctx.enter_context(nc.psum_tensor(name, shape, f32))

        def sem(name):
            return ctx.enter_context(nc.semaphore(name))

        X = sb("X", [P, UNITS, NQ, BLK], f32)
        N0 = sb("N0", [P, W + BC * NI * N0STR + W], f32)
        U = sb("U", [P, BLK], f32)
        UH = sb("UH", [P, BLK], f16)
        UL = sb("UL", [P, BLK], f16)
        N1 = sb("N1", [P, BLK], f32)
        H1 = sb("H1", [P, 2, NPAD], f16)
        L1 = sb("L1", [P, 2, NPAD], f16)
        HK = sb("HK", [P, 2, ROW], f16)
        WT = sb("WT", [P, GC, TAPS, P], f16)
        MY = sb("MY", [P, NQ, 2, P], f16)
        C0 = sb("C0", [P, NQ, 4], f32)
        C1 = sb("C1", [P, NQ, BC, 4], f32)
        PAR = sb("PAR", [P, P], f32)
        BN = [sb("BN0", [P, NI, NQ, 6], f32), sb("BN1", [P, NI, NQ, 6], f32)]
        SQ = [sb("SQ0", [P, NI * NQ * 2], f32), sb("SQ1", [P, NI * NQ * 2], f32)]
        SUMS = [sb("SUMS0", [P, 2 * NI], f32), sb("SUMS1", [P, 2 * NI], f32)]
        MOM = [sb("MOM0", [P, 4 * NI], f32), sb("MOM1", [P, 4 * NI], f32)]
        COEF = [sb("COEF0", [P, NH, 2 * NI], f32), sb("COEF1", [P, NH, 2 * NI], f32)]

        ps_l0 = pb("ps_l0", [P, BC * NP])
        ps_l1 = [pb(f"ps_l1_{n}", [P, NP]) for n in range(3)]
        ps_sum = pb("ps_sum", [P, 2, 2 * NI])

        room = WT[:, :, :, :].rearrange("p a b c -> p (a b c)")
        PCH = 8
        f = P * PCH * 2
        DIFF = room[:, 0:f].bitcast(f32).rearrange("p (n m) -> p n m", n=PCH)
        TMP = room[:, f:2 * f].bitcast(f32).rearrange("p (n m) -> p n m", n=PCH)
        ACC = room[:, 2 * f:3 * f].bitcast(f32).rearrange("p (n m) -> p n m", n=PCH)
        MHL = room[:, 3 * f:4 * f].rearrange("p (n k m) -> p n k m", n=PCH, k=2)
        GT = room[0:CP, 4 * f:4 * f + CT * ROW].rearrange("p (t a m) -> p t a m", t=CT, a=TAPS)
        ZERO = sb("ZERO", [1, P], f16)
        small = {}
        for name, n in (("w77", K * K), ("w53", 15), ("w35", 15), ("w7w", 7), ("w7h", 7), ("w5w", 5),
                        ("w5h", 5), ("b77", 1), ("b53", 1), ("b35", 1)):
            small[name] = sb("in_" + name, [CP, CT, n], f32)
        KK = sb("KK", [CP, CT, K * K], f32)
        KT = sb("KT", [CP, CT, K * K], f32)
        KH = sb("KH", [CP, CT, K * K], f16)
        KM = sb("KM", [CP, CT, 1], f32)
        KI = sb("KI", [CP, CT, 1], f32)
        KS = sb("KS", [CP, CT, 1], f32)
        KC = sb("KC", [CP, CT, 4], f32)
        OFF = sb("OFF", [P, 2 * NPOS], f32)
        RND = sb("RND", [P, 2 * NPOS], f32)
        FRAC = sb("FRAC", [P, 2 * NPOS], f32)
        DSQ = sb("DSQ", [P, 3, 2 * NPOS], f32)
        EX = sb("EX", [P, 3, 2 * NPOS], f32)
        NRM = sb("NRM", [P, 4, NPOS], f32)
        TY = sb("TY", [P, 3, NPOS], f32)
        CC = sb("CC", [P, NPOS, 4], f32)
        ROWID = sb("ROWID", [P, NPOS], f32)
        PIDX = sb("PIDX", [P, 1], f32)
        MIDX = sb("MIDX", [P, P], f32)
        PMIDX = sb("PMIDX", [P, P], i32)

        x_loaded = [sem(f"x_loaded{n}") for n in range(PERIOD)]
        stored = [sem(f"stored{n}") for n in range(PERIOD)]
        l0_matrix_loaded = [sem(f"l0_matrix_loaded{n}") for n in range(NQ)]
        l1_coef_loaded = [sem(f"l1_coef_loaded{n}") for n in range(NQ)]
        hankel_loaded = [sem(f"hankel_loaded{n}") for n in range(2)]
        small_loaded = sem("small_loaded")
        offset_loaded = sem("offset_loaded")
        index_ready = sem("index_ready")
        pads_ready = sem("pads_ready")
        prep = sem("prep")
        exps_in = sem("exps_in")
        exps_ready = sem("exps_ready")
        parity_ready = sem("parity_ready")
        chunk_ready = sem("chunk_ready")
        chunk_stored = sem("chunk_stored")
        tables_ready = sem("tables_ready")
        prologue_done = sem("prologue_done")
        l0_coef_ready = sem("l0_coef_ready")
        scratch_stored = sem("scratch_stored")
        n0_ready = sem("n0_ready")
        taps_part = sem("taps_part")
        u_ready = sem("u_ready")
        uh_ready = sem("uh_ready")
        ul_ready = sem("ul_ready")
        l0_done = sem("l0_done")
        x1_ready = sem("x1_ready")
        bn_done = [sem("bn0_done"), sem("bn1_done")]
        chain = [sem("chain0"), sem("chain1")]
        sums_ready = [sem("sums0_ready"), sem("sums1_ready")]
        sums_done = [sem("sums0_done"), sem("sums1_done")]
        var_ready = [sem("var0_ready"), sem("var1_ready")]
        scale_ready = [sem("scale0_ready"), sem("scale1_ready")]
        coef_ready = [sem("coef0_ready"), sem("coef1_ready")]
        n1_ready = sem("n1_ready")
        h1_ready = sem("h1_ready")
        l1_ready = sem("l1_ready")
        matrix_ready = sem("matrix_ready")
        conv_done = sem("conv_done")
        z_ready = sem("z_ready")
        out_ready = sem("out_ready")

        CHAIN = 6

        def slots(eng, g):
            if isinstance(g, int):
                return [(2 * g + d) % UNITS for d in range(UNITS)]
            return [eng.snap((address(g) * 2 + d) % UNITS) for d in range(UNITS)]

        def xblock(slot, g, k):
            s = slot[(k // NQ) % UNITS]
            return X[:, bass.ds(s, 1), k % NQ, :].rearrange("p a n -> p (a n)")

        def blocks(eng, body, last):
            body(0, range(PERIOD))
            with eng.Fori(0, NG - 2) as g:
                body(Count(g, 1, 1), range(PERIOD))
            body(NG - 1, range(PERIOD + last))

        def live(g, k):
            return not isinstance(g, int) or 0 <= g * PERIOD + k < NBLOCKS

        def holder(eng):
            product = eng.alloc_register(f"product_{eng.engine.name}")
            count = eng.alloc_register(f"count_{eng.engine.name}")

            def hold(s, value):
                if isinstance(value, int):
                    eng.wait_ge(s, value)
                    return
                eng.reg_mul(product, value.g, value.a)
                eng.reg_add(count, product, value.b)
                eng.wait_ge(prologue_done, 1)
                eng.wait_ge(s, count)
            return hold

        def unfolded(g, k):
            return [((k - d) // PERIOD, (k - d) % PERIOD * BC + c) for d, c0 in ((3, 2), (2, 0)) for c in (c0, c0 + 1)
                    if live(g, k - d) and (k - d) % PERIOD < NQ]

        def images(t, k):
            return t[:, k % 2, 4:4 + BC * NI * ISTR].rearrange("p (n x) -> p n x", x=ISTR)[:, :, 0:W]

        block = ctx.enter_context(nc.Block())

        @block.sync
        def _(sp):
            hold = holder(sp)
            sp.dma_start(OFF[:, :], offset.rearrange("n k -> (n k)").partition_broadcast(P))\
                .then_inc(offset_loaded, 16)
            flat = {"w77": w77, "w53": w53, "w35": w35, "w7w": w7w, "w7h": w7h, "w5w": w5w, "w5h": w5h}
            for name, w in flat.items():
                sp.dma_start(small[name][:, :, :], w.rearrange("(t p) a h w -> p t (a h w)", p=CP))\
                    .then_inc(small_loaded, 16)
            with nc.allow_non_contiguous_dma(reason="a few hundred biases"):
                for name, b in (("b77", b77), ("b53", b53), ("b35", b35)):
                    sp.dma_start(small[name][:, :, :], b.rearrange("(t p k) -> p t k", p=CP, k=1))\
                        .then_inc(small_loaded, 16)

            def load_x(g, k):
                dk = k % PERIOD
                gg = g + k // PERIOD
                if live(g, k - UNITS * NQ):
                    old = k - UNITS * NQ
                    hold(stored[old % PERIOD], DMAS * (g + old // PERIOD + 1))
                dst = xblock(s3, g, k)
                for c in range(BC):
                    for r in range(2):
                        sp.dma_start(dst[r::2, c * NP:(c + 1) * NP].rearrange("p (i x) -> p i x", i=NI),
                                     x_v[bass.ds(address(gg), 1), dk % NQ, c, dk // NQ, r].rearrange("g y i x -> (g y) i x"))\
                            .then_inc(x_loaded[dk], 16)

            def store(g, k):
                dk = k % PERIOD
                gg = g + k // PERIOD
                src = xblock(s3, g, k)
                hold(out_ready, (g * PERIOD + k + 1) * BC)
                for c in range(BC):
                    for r in range(2):
                        sp.dma_start(out_v[bass.ds(address(gg), 1), dk % NQ, c, dk // NQ, r].rearrange("g y i x -> (g y) i x"),
                                     src[r::2, c * NP:(c + 1) * NP].rearrange("p (i x) -> p i x", i=NI))\
                            .then_inc(stored[dk], 16)

            def load_l0(g, q):
                if not isinstance(g, int) or g > 0:
                    hold(l0_done, 2 * (g * PERIOD - NQ + q + 1))
                n = g * NQ + q
                sp.dma_start(MY[:, q, :, :].rearrange("p k m -> p (k m)"),
                             shift_v[bass.ds(address(n), 1), :, :].rearrange("n p m -> (n p) m"))\
                    .then_inc(l0_matrix_loaded[q], 16)
                sp.dma_start(C0[:, q, :], bass.AP(tensor=l0_coef_v.tensor, offset=address(n * 4), ap=[[0, P], [1, 4]]))\
                    .then_inc(l0_matrix_loaded[q], 16)

            def load_l1_coef(g, q):
                if not isinstance(g, int) or g > 0:
                    hold(out_ready, (g * PERIOD - NQ + q + 1) * BC)
                sp.dma_start(C1[:, q, :, :].rearrange("p c k -> p (c k)"),
                             bass.AP(tensor=l1_coef_d.tensor, offset=address((g * NQ + q) * BC * 4),
                                     ap=[[0, P], [1, BC * 4]])).then_inc(l1_coef_loaded[q], 16)

            def load_hankel(g, c):
                n = g * GC + c
                if not isinstance(g, int) or n >= 2:
                    hold(matrix_ready, n - 1)
                sp.dma_start(HK[:, c % 2, :],
                             bass.AP(tensor=hankel_d.tensor, offset=address(n * ROW), ap=[[1, P], [1, ROW]]))\
                    .then_inc(hankel_loaded[c % 2], 16)

            s3 = slots(sp, 0)
            for k in range(4):
                load_x(0, k)
            for n in range(NPOS // PCH if NPOS % PCH == 0 else NPOS // PCH + 1):
                m = min(PCH, NPOS - n * PCH)
                sp.wait_ge(chunk_ready, n + 1)
                for d in range(2):
                    sp.dma_start(shift_d[n * PCH:n * PCH + m, d].rearrange("n p m -> p n m"),
                                 MHL[:, 0:m].rearrange("p n k m -> p n (k m)")).then_inc(chunk_stored, 16)
            chunks = (NPOS + PCH - 1) // PCH
            sp.wait_ge(l0_coef_ready, 1)
            with nc.allow_non_contiguous_dma(reason="a few coefficients"):
                for d in range(2):
                    sp.dma_start(l0_coef_d[:, d, :], CC[0:1, :, :]).then_inc(scratch_stored, 16)
            sp.wait_ge(tables_ready, 1)
            sp.dma_start(hankel_d[0:C * ROW].rearrange("(t p n) -> p t n", p=CP, n=ROW),
                         GT[:, :, :, :].rearrange("p t a m -> p t (a m)")).then_inc(scratch_stored, 16)
            sp.dma_start(hankel_d[C * ROW:C * ROW + P].rearrange("(a n) -> a n", a=1), ZERO[:, :])\
                .then_inc(scratch_stored, 16)
            sp.dma_start(l1_coef_d.rearrange("(t p) k -> p t k", p=CP), KC[:, :, :]).then_inc(scratch_stored, 16)
            sp.wait_ge(chunk_stored, 32 * chunks)
            sp.wait_ge(scratch_stored, 16 * 5)
            for q in range(2):
                load_l0(0, q)
            for c in range(2):
                load_hankel(0, c)

            def steps(g, ks):
                nonlocal s3
                s3 = slots(sp, g)
                for k in ks:
                    if live(g, k - LAG - 1):
                        store(g, k - LAG - 1)
                    if live(g, k + 2) and (k + 2) % PERIOD < NQ:
                        load_l0(g + (k + 2) // PERIOD, (k + 2) % PERIOD)
                    if live(g, k - 2) and (k - 2) % PERIOD < NQ:
                        load_l1_coef(g + (k - 2) // PERIOD, (k - 2) % PERIOD)
                    for d, c in unfolded(g, k)[2:]:
                        load_hankel(g + d, c)
                    if live(g, k + 4):
                        load_x(g, k + 4)
                    for d, c in unfolded(g, k + 1)[:2]:
                        if isinstance(g, Count) or (g, k) != (0, 1):
                            load_hankel(g + d, c)

            blocks(sp, steps, LAG + 1)
            for n in range(PERIOD):
                sp.wait_ge(stored[n], DMAS * NG)

        @block.gpsimd
        def _(pool):
            hold = holder(pool)
            pool.iota(PIDX[:, :], [[0, 1]], base=0, channel_multiplier=1,
                      allow_small_or_imprecise_dtypes=True).then_inc(index_ready, 1)
            pool.iota(MIDX[:, :], [[1, P]], base=0, channel_multiplier=0,
                      allow_small_or_imprecise_dtypes=True).then_inc(index_ready, 1)
            pool.iota(PMIDX[:, :], [[1, P]], base=0, channel_multiplier=1).then_inc(index_ready, 1)
            pool.memset(N0[:, :], 0.0).then_inc(pads_ready, 1)
            pool.memset(H1[:, :, :], 0.0).then_inc(pads_ready, 1)
            pool.memset(L1[:, :, :], 0.0).then_inc(pads_ready, 1)
            pool.wait_ge(pads_ready, 3)

            def steps(g, ks):
                for k in ks:
                    if live(g, k):
                        hold(uh_ready, g * PERIOD + k + 1)
                        if live(g, k - 1):
                            hold(l0_done, 2 * (g * PERIOD + k))
                        pool.tensor_tensor(UL[:, :], U[:, :], UH[:, :], ALU.subtract).then_inc(ul_ready, 1)
                    kb = k - LAG + 1
                    if live(g, kb):
                        hold(h1_ready, g * PERIOD + kb + 1)
                        if live(g, kb - 2):
                            hold(conv_done, (g * PERIOD + kb - 1) * BC)
                        pool.tensor_tensor(images(L1, kb), N1[:, :].rearrange("p (n x) -> p n x", x=W),
                                           images(H1, kb), ALU.subtract).then_inc(l1_ready, 1)

            blocks(pool, steps, LAG)

        @block.scalar
        def _(act):
            hold = holder(act)
            act.wait_ge(exps_in, 1)
            act.activation(EX[:, :, :], DSQ[:, :, :], EXP, scale=-2.0).then_inc(exps_ready, 1)
            act.wait_ge(pads_ready, 3)

            def normalise(g, k, kind, dst, done):
                src = xblock(s3, g, k).rearrange("p (c i x) -> p c i x", c=BC, i=NI)
                h = (k // NQ) % NH
                for i in range(NI):
                    ins = act.activation(dst[:, :, i, :], src[:, :, i, :], IDENT,
                                         scale=COEF[kind][:, h, i:i + 1], bias=COEF[kind][:, h, NI + i:NI + i + 1])
                ins.then_inc(done, 1)

            def root(g, k, kind):
                unit, h = g * NH + k // NQ, (k // NQ) % NH
                hold(var_ready[kind], unit + 1)
                act.activation(COEF[kind][:, h, 0:NI], MOM[kind][:, 3 * NI:4 * NI], SQRT, scale=ACT_SCALE ** 2)\
                    .then_inc(scale_ready[kind], 1)

            def result(g, k, c):
                hold(z_ready, (g * PERIOD + k) * BC + c + 1)
                v = xblock(s3, g, k)[:, c * NP:(c + 1) * NP]
                q = k % NQ
                act.activation(v, v, IDENT, scale=C1[:, q, c, 1:2], bias=C1[:, q, c, 2:3]).then_inc(out_ready, 1)

            n0_images = N0[:, W:W + BC * NI * N0STR].rearrange("p (c i x) -> p c i x", c=BC, i=NI)[:, :, :, 0:W]
            n1_images = N1[:, :].rearrange("p (c i x) -> p c i x", c=BC, i=NI)

            def normalise_l0(g, k):
                hold(coef_ready[0], g * NH + k // NQ + 1)
                if live(g, k - 1):
                    hold(u_ready, g * PERIOD + k)
                normalise(g, k, 0, n0_images, n0_ready)

            def steps(g, ks):
                nonlocal s3
                s3 = slots(act, g)
                for k in ks:
                    if live(g, k - LAG - 1):
                        result(g, k - LAG - 1, 3)
                    if live(g, k):
                        hold(u_ready, g * PERIOD + k + 1)
                        if live(g, k - 1):
                            hold(l0_done, 2 * (g * PERIOD + k))
                        act.activation(UH[:, :], U[:, :], IDENT).then_inc(uh_ready, 1)
                    if live(g, k - 1) and (k - 1) % NQ == NQ - 1:
                        root(g, k - 1, 1)
                    if live(g, k - LAG):
                        result(g, k - LAG, 0)
                    kb = k - LAG + 1
                    if live(g, kb):
                        hold(coef_ready[1], g * NH + kb // NQ + 1)
                        if live(g, kb - 1):
                            hold(l1_ready, g * PERIOD + kb)
                        normalise(g, kb, 1, n1_images, n1_ready)
                        hold(n1_ready, g * PERIOD + kb + 1)
                        if live(g, kb - 2):
                            hold(conv_done, (g * PERIOD + kb - 1) * BC)
                        act.activation(images(H1, kb), N1[:, :].rearrange("p (n x) -> p n x", x=W), IDENT)\
                            .then_inc(h1_ready, 1)
                    if live(g, k - LAG):
                        result(g, k - LAG, 1)
                    if live(g, k + 3) and (k + 3) % NQ == NQ - 1:
                        root(g, k + 3, 0)
                    if live(g, k + 1):
                        normalise_l0(g, k + 1)
                    if live(g, k - LAG):
                        result(g, k - LAG, 2)

            s3 = slots(act, 0)
            root(0, 0, 0)
            normalise_l0(0, 0)
            blocks(act, steps, LAG + 1)

        @block.vector
        def _(dve):
            hold = holder(dve)
            count = [0]

            def step(ins):
                count[0] += 1
                ins.then_inc(prep, 1)
                dve.wait_ge(prep, count[0])

            dve.wait_ge(offset_loaded, 16)
            step(dve.tensor_scalar(OFF[:, :], OFF[:, :], -1000.0, 1000.0, ALU.max, ALU.min))
            step(dve.tensor_scalar(RND[:, :], OFF[:, :], 12582912.0, None, ALU.add))
            step(dve.tensor_scalar(RND[:, :], RND[:, :], -12582912.0, None, ALU.add))
            step(dve.tensor_tensor(FRAC[:, :], OFF[:, :], RND[:, :], ALU.subtract))
            for t in range(3):
                step(dve.tensor_scalar(DSQ[:, t, :], FRAC[:, :], float(t - 1), None, ALU.add))
            for t in range(3):
                ins = dve.tensor_tensor(DSQ[:, t, :], DSQ[:, t, :], DSQ[:, t, :], ALU.mult)
            step(ins)
            dve.nop().then_inc(exps_in, 1)
            dve.wait_ge(index_ready, 3)
            step(dve.tensor_scalar(PMIDX[:, :], PMIDX[:, :], 1, None, ALU.bitwise_and))
            dve.tensor_scalar(PAR[:, :], PMIDX[:, :], 0.0, None, ALU.is_equal).then_inc(parity_ready, 1)
            dve.wait_ge(exps_ready, 1)
            ex = EX[:, :, :].rearrange("p t (n k) -> p t k n", k=2)
            rnd = RND[:, :].rearrange("p (n k) -> p k n", k=2)
            for k in range(2):
                step(dve.tensor_tensor(NRM[:, k, :], ex[:, 0, k, :], ex[:, 1, k, :], ALU.add))
                step(dve.tensor_tensor(NRM[:, k, :], NRM[:, k, :], ex[:, 2, k, :], ALU.add))
            step(dve.tensor_tensor(NRM[:, 2, :], NRM[:, 0, :], NRM[:, 1, :], ALU.mult))
            step(dve.reciprocal(NRM[:, 2, :], NRM[:, 2, :]))
            step(dve.scalar_tensor_tensor(NRM[:, 2, :], NRM[:, 2, :], L0_SCALE, ex[:, 1, 0, :], ALU.mult, ALU.mult))
            for t in range(3):
                dve.tensor_tensor(TY[:, t, :], ex[:, t, 1, :], NRM[:, 2, :], ALU.mult)
            step(dve.reciprocal(NRM[:, 3, :], ex[:, 1, 0, :]))
            dve.tensor_tensor(CC[:, :, 0], ex[:, 0, 0, :], NRM[:, 3, :], ALU.mult)
            dve.tensor_tensor(CC[:, :, 1], ex[:, 2, 0, :], NRM[:, 3, :], ALU.mult)
            step(dve.tensor_scalar(NRM[:, 0, :], rnd[:, 0, :], float(-W), float(W), ALU.max, ALU.min))
            step(dve.tensor_scalar(NRM[:, 0, :], NRM[:, 0, :], -1.0, float(W), ALU.mult, ALU.add))
            dve.tensor_copy(CC[:, :, 2].bitcast(i32), NRM[:, 0, :])
            step(dve.memset(CC[:, :, 3], 0.0))
            dve.nop().then_inc(l0_coef_ready, 1)
            step(dve.tensor_scalar(ROWID[:, :], rnd[:, 1, :], 2.0, PIDX[:, 0:1], ALU.mult, ALU.add))
            step(dve.tensor_scalar(NRM[:, 0, :], ROWID[:, :], 0.0, None, ALU.is_ge))
            step(dve.tensor_scalar(NRM[:, 1, :], ROWID[:, :], float(P - 1), None, ALU.is_le))
            step(dve.tensor_tensor(NRM[:, 0, :], NRM[:, 0, :], NRM[:, 1, :], ALU.mult))
            step(dve.tensor_scalar(ROWID[:, :], ROWID[:, :], 1000.0, None, ALU.add))
            step(dve.tensor_tensor(ROWID[:, :], ROWID[:, :], NRM[:, 0, :], ALU.mult))
            step(dve.tensor_scalar(ROWID[:, :], ROWID[:, :], -1000.0, None, ALU.add))
            for n in range((NPOS + PCH - 1) // PCH):
                m = min(PCH, NPOS - n * PCH)
                at = slice(n * PCH, n * PCH + m)

                def wide(v):
                    return v.rearrange("p (n m) -> p n m", m=1).to_broadcast([P, m, P])
                cols = MIDX[:, :].rearrange("p (n m) -> p n m", n=1).to_broadcast([P, m, P])
                step(dve.tensor_tensor(DIFF[:, 0:m, :], wide(ROWID[:, at]), cols, ALU.subtract))
                for t in range(3):
                    dst = ACC if t == 0 else TMP
                    step(dve.scalar_tensor_tensor(dst[:, 0:m, :], DIFF[:, 0:m, :], float(2 * (t - 1)),
                                                  wide(TY[:, t, at]), ALU.is_equal, ALU.mult))
                    if t > 0:
                        step(dve.tensor_tensor(ACC[:, 0:m, :], ACC[:, 0:m, :], TMP[:, 0:m, :], ALU.add))
                if n > 0:
                    dve.wait_ge(chunk_stored, 32 * n)
                step(dve.tensor_copy(MHL[:, 0:m, 0, :], ACC[:, 0:m, :]))
                step(dve.tensor_tensor(MHL[:, 0:m, 1, :], ACC[:, 0:m, :], MHL[:, 0:m, 0, :], ALU.subtract))
                dve.nop().then_inc(chunk_ready, 1)
            dve.wait_ge(small_loaded, 16 * 10)
            dve.memset(ZERO[:, :], 0.0)
            step(dve.memset(GT, 0.0))
            for t in range(CT):
                kk = KK[:, t, :].rearrange("p (i j) -> p i j", i=K)
                kt = KT[:, t, :].rearrange("p (i j) -> p i j", i=K)

                def col(name, n):
                    return small[name][:, t, :].rearrange("p (i j) -> p i j", j=1).to_broadcast([CP, n, n])

                def row(name, n):
                    return small[name][:, t, :].rearrange("p (i j) -> p i j", i=1).to_broadcast([CP, n, n])
                step(dve.tensor_tensor(kt, col("w7h", 7), row("w7w", 7), ALU.mult))
                step(dve.tensor_tensor(kk, kt, small["w77"][:, t, :].rearrange("p (i j) -> p i j", i=K), ALU.add))
                for name, i0, ni, nj in (("w53", 1, 5, 3), ("w35", 2, 3, 5)):
                    j0 = R - nj // 2
                    v = kk[:, i0:i0 + ni, j0:j0 + nj]
                    step(dve.tensor_tensor(v, v, small[name][:, t, :].rearrange("p (i j) -> p i j", i=ni), ALU.add))
                step(dve.tensor_tensor(kt[:, 1:6, 1:6], col("w5h", 5), row("w5w", 5), ALU.mult))
                step(dve.tensor_tensor(kk[:, 1:6, 1:6], kk[:, 1:6, 1:6], kt[:, 1:6, 1:6], ALU.add))
            step(dve.tensor_reduce(KM[:, :, :], KK[:, :, :], AX.X, ALU.max, apply_absolute_value=True))
            step(dve.tensor_scalar(KM[:, :, :], KM[:, :, :], 1e-18, None, ALU.max))
            kmi = KM[:, :, :].bitcast(i32)
            step(dve.tensor_scalar(kmi, kmi, 0x7F800000, None, ALU.bitwise_and))
            step(dve.tensor_scalar(KI[:, :, :], KM[:, :, :], 1.0 / KTOP, None, ALU.mult))
            step(dve.reciprocal(KS[:, :, :], KI[:, :, :]))
            dve.tensor_scalar(KC[:, :, 0:1], KS[:, :, :], ACT_SCALE, None, ALU.mult)
            dve.tensor_scalar(KC[:, :, 1:2], KI[:, :, :], 1.0 / ACT_SCALE, None, ALU.mult)
            step(dve.tensor_tensor(KC[:, :, 2:3], small["b77"][:, :, :], small["b53"][:, :, :], ALU.add))
            step(dve.tensor_tensor(KC[:, :, 2:3], KC[:, :, 2:3], small["b35"][:, :, :], ALU.add))
            dve.memset(KC[:, :, 3:4], 0.0)
            step(dve.tensor_tensor(KK[:, :, :], KK[:, :, :], KS[:, :, :].to_broadcast([CP, CT, K * K]), ALU.mult))
            step(dve.tensor_copy(KH[:, :, :], KK[:, :, :]))
            step(dve.tensor_tensor(KT[:, :, :], KK[:, :, :], KH[:, :, :], ALU.subtract))
            for t in range(CT):
                for i in range(K):
                    at = FIRST + 2 * i
                    dve.tensor_copy(GT[:, t, 0:K, at], KH[:, t, i * K:(i + 1) * K])
                    ins = dve.tensor_copy(GT[:, t, K:TAPS, at], KT[:, t, i * K:(i + 1) * K])
            ins.then_inc(tables_ready, 1)
            dve.nop().then_inc(prologue_done, 1)

            def statistics(g, k, kind):
                if kind == 0:
                    hold(x_loaded[k % PERIOD], DMAS * (g + k // PERIOD + 1))
                else:
                    hold(x1_ready, 2 * (g * PERIOD + k + 1))
                src = xblock(s3, g, k).rearrange("p (c i x) -> p c i x", c=BC, i=NI)
                for i in range(NI):
                    ins = dve.bn_stats(BN[kind][:, i, k % NQ, :], src[:, :, i, :])
                ins.then_inc(bn_done[kind], 1)

            def links(unit, kind, n):
                def link(ins):
                    nonlocal n
                    n += 1
                    ins.then_inc(chain[kind], 1)
                    hold(chain[kind], unit * CHAIN + n)
                return link

            def row_sums(g, k, kind):
                unit = g * NH + k // NQ
                link = links(unit, kind, 0)
                cnt = BC * W / 2
                tup = BN[kind][:, :, :, :].rearrange("p i q (e v) -> p (i q e) v", v=3)
                hold(bn_done[kind], (unit + 1) * NQ)
                link(dve.scalar_tensor_tensor(SQ[kind][:, :], tup[:, :, 1], cnt, tup[:, :, 1], ALU.mult, ALU.mult))
                link(dve.tensor_tensor(SQ[kind][:, :], SQ[kind][:, :], tup[:, :, 2], ALU.add))
                dve.tensor_reduce(SUMS[kind][:, 0:NI], tup[:, :, 1].rearrange("p (i n) -> p i n", n=2 * NQ),
                                  AX.X, ALU.add)
                dve.tensor_reduce(SUMS[kind][:, NI:2 * NI], SQ[kind][:, :].rearrange("p (i n) -> p i n", n=2 * NQ),
                                  AX.X, ALU.add).then_inc(sums_ready[kind], 1)

            def variances(g, k, kind):
                unit = g * NH + k // NQ
                link = links(unit, kind, 2)
                mean, sq, var, rs = (MOM[kind][:, j * NI:(j + 1) * NI] for j in range(4))
                hold(sums_done[kind], unit + 1)
                link(dve.tensor_scalar(mean, ps_sum[:, kind, 0:NI], 1.0 / (H * 2 * NQ), None, ALU.mult))
                link(dve.tensor_tensor(sq, mean, mean, ALU.mult))
                link(dve.scalar_tensor_tensor(var, ps_sum[:, kind, NI:2 * NI], 1.0 / (GC * H * W), sq,
                                              ALU.mult, ALU.subtract))
                link(dve.tensor_scalar(rs, var, 0.0, EPS, ALU.max, ALU.add))
                dve.reciprocal(rs, rs).then_inc(var_ready[kind], 1)

            def shifts(g, k, kind):
                unit = g * NH + k // NQ
                h = (k // NQ) % NH
                mean, scale, shift = MOM[kind][:, 0:NI], COEF[kind][:, h, 0:NI], COEF[kind][:, h, NI:2 * NI]
                hold(scale_ready[kind], unit + 1)
                dve.scalar_tensor_tensor(shift, mean, -1.0, scale, ALU.mult, ALU.mult)\
                    .then_inc(coef_ready[kind], 1)

            def unfold(g, c):
                n = g * GC + c
                hold(hankel_loaded[c % 2], 16 * (g * (GC // 2) + c // 2 + 1))
                if not isinstance(g, int) or g > 0:
                    hold(conv_done, (g * PERIOD - NQ) * BC + c + 1)
                dve.tensor_copy(WT[:, c, :, :],
                                 HK[:, c % 2, :].rearrange("p (a m) -> p a m", a=TAPS)[:, :, P - 1::-1])\
                    .then_inc(matrix_ready, 1)

            def taps_x(g, k):
                q = k % NQ
                hold(l0_matrix_loaded[q], 32 * (g + 1))
                at = dve.value_load(C0[0:1, q, 2:3].bitcast(i32), min_val=0, max_val=2 * W)
                hold(n0_ready, g * PERIOD + k + 1)
                if live(g, k - 1):
                    hold(ul_ready, g * PERIOD + k)
                v = N0[:, bass.ds(at, BC * NI * N0STR)].rearrange("p (n x) -> p n x", x=N0STR)
                u = U[:, :].rearrange("p (n x) -> p n x", x=W)
                dve.tensor_copy(u[:, :, 0:1], v[:, :, 0:1])
                dve.scalar_tensor_tensor(u[:, :, 1:W], v[:, :, 0:W - 1], C0[:, q, 0:1], v[:, :, 1:W],
                                         ALU.mult, ALU.add).then_inc(taps_part, 1)
                hold(taps_part, g * PERIOD + k + 1)
                dve.scalar_tensor_tensor(u[:, :, 0:W - 1], v[:, :, 1:W], C0[:, q, 1:2], u[:, :, 0:W - 1],
                                         ALU.mult, ALU.add).then_inc(u_ready, 1)

            def evacuate(g, k):
                dst = xblock(s3, g, k)
                for n in range(2):
                    hold(l0_done, 2 * (g * PERIOD + k) + n + 1)
                    v = dst[:, n * 2 * NP:(n + 1) * 2 * NP]
                    dve.scalar_tensor_tensor(v, ps_l0[:, n * 2 * NP:(n + 1) * 2 * NP], 1.0 / (ACT_SCALE * L0_SCALE),
                                             v, ALU.mult, ALU.add).then_inc(x1_ready, 1)

            def residual(g, k, c):
                q = k % NQ
                if c == 0:
                    hold(l1_coef_loaded[q], 16 * (g + k // PERIOD + 1))
                hold(conv_done, (g * PERIOD + k) * BC + c + 1)
                v = xblock(s3, g, k)[:, c * NP:(c + 1) * NP]
                dve.scalar_tensor_tensor(v, v, C1[:, q, c, 0:1], ps_l1[(k + c) % 3][:, :], ALU.mult, ALU.add)\
                    .then_inc(z_ready, 1)

            def steps(g, ks):
                nonlocal s3
                s3 = slots(dve, g)
                for k in ks:
                    old, new = k - LAG - 1, k - LAG
                    matrices = unfolded(g, k)
                    early = len(matrices) - 2
                    ends1 = live(g, k - 1) and (k - 1) % NQ == NQ - 1
                    ends0 = live(g, k + 3) and (k + 3) % NQ == NQ - 1
                    if live(g, old):
                        residual(g, old, 3)
                    if live(g, k):
                        taps_x(g, k)
                    if ends1:
                        variances(g, k - 1, 1)
                    if live(g, new):
                        residual(g, new, 0)
                    if ends1:
                        shifts(g, k - 1, 1)
                    if live(g, k + 3):
                        statistics(g, k + 3, 0)
                        if ends0:
                            row_sums(g, k + 3, 0)
                    for d, c in matrices[0:early]:
                        unfold(g + d, c)
                    if live(g, new):
                        residual(g, new, 1)
                    if ends0:
                        variances(g, k + 3, 0)
                    if live(g, new):
                        residual(g, new, 2)
                    for d, c in matrices[max(early, 0):]:
                        unfold(g + d, c)
                    if ends0:
                        shifts(g, k + 3, 0)
                    if live(g, k):
                        evacuate(g, k)
                        statistics(g, k, 1)
                        if k % NQ == NQ - 1:
                            row_sums(g, k, 1)

            s3 = slots(dve, 0)
            for k in range(3):
                statistics(0, k, 0)
            row_sums(0, NQ - 1, 0)
            variances(0, NQ - 1, 0)
            shifts(0, NQ - 1, 0)
            blocks(dve, steps, LAG + 1)

        @block.tensor
        def _(pe):
            hold = holder(pe)
            pe.wait_ge(parity_ready, 1)

            def sums(g, k, kind):
                hold(sums_ready[kind], g * NH + k // NQ + 1)
                pe.matmul(ps_sum[:, kind, :], PAR[:, :], SUMS[kind][:, :], start=True, stop=True)\
                    .then_inc(sums_done[kind], 1)

            def l0(g, k):
                q = k % NQ
                hold(ul_ready, g * PERIOD + k + 1)
                hold(uh_ready, g * PERIOD + k + 1)
                hold(l0_matrix_loaded[q], 32 * (g + 1))
                for n in range(2):
                    if live(g, k - 1):
                        hold(x1_ready, 2 * (g * PERIOD + k) - 1 + n)
                    for c in (2 * n, 2 * n + 1):
                        cols = slice(c * NP, (c + 1) * NP)
                        for j, (m, v) in enumerate(((0, UH), (0, UL), (1, UH))):
                            ins = pe.matmul(ps_l0[:, cols], MY[:, q, m, :], v[:, cols], start=(j == 0), stop=(j == 2))
                    ins.then_inc(l0_done, 1)

            def l1(g, k, c, parts=range(3)):
                gg, q = g + k // PERIOD, k % NQ
                ch = q * BC + c
                n = (g * PERIOD + k) * BC + c
                if 0 in parts:
                    if c == 0:
                        hold(h1_ready, g * PERIOD + k + 1)
                        hold(l1_ready, g * PERIOD + k + 1)
                    hold(matrix_ready, gg * GC + ch + 1)
                    if not isinstance(n, int) or n >= 3:
                        hold(z_ready, n - 2)
                ps = ps_l1[(k + c) % 3][:, :].rearrange("p (i x) -> p i x", i=NI)
                last = 3 * K - 1
                for t in range(parts[0] * K, (parts[-1] + 1) * K):
                    j, part = t % K, t // K
                    src = (H1, H1, L1)[part]
                    low = K if part == 1 else 0
                    at = 4 + c * NI * ISTR + j - R
                    v = src[:, k % 2, at:at + NI * ISTR].rearrange("p (i x) -> p i x", i=NI)[:, :, 0:W]
                    ins = pe.matmul(ps, WT[:, ch, low + j, :], v, start=(t == 0), stop=(t == last))
                if parts[-1] == 2:
                    ins.then_inc(conv_done, 1)

            def steps(g, ks):
                for k in ks:
                    old = k - LAG
                    if live(g, old):
                        l1(g, old, 0, (0,))
                    if live(g, k - 1) and (k - 1) % NQ == NQ - 1:
                        sums(g, k - 1, 1)
                    if live(g, old):
                        l1(g, old, 0, (1, 2))
                        l1(g, old, 1)
                        l1(g, old, 2, (0, 1))
                    if live(g, k + 3) and (k + 3) % NQ == NQ - 1:
                        sums(g, k + 3, 0)
                    if live(g, old):
                        l1(g, old, 2, (2,))
                    if live(g, k):
                        l0(g, k)
                    if live(g, old):
                        l1(g, old, 3)

            sums(0, NQ - 1, 0)
            blocks(pe, steps, LAG)


_INS = ["x", "L0_conv_offset", "L1_conv_w77", "L1_conv_b77", "L1_conv_w53", "L1_conv_b53", "L1_conv_w35",
        "L1_conv_b35", "L1_conv_w7w", "L1_conv_w7h", "L1_conv_w5w", "L1_conv_w5h"]


def kernel(**inputs):
    import numpy as _np
    import concourse.bacc as _bacc
    from concourse import mybir as _mybir
    from concourse.bass_utils import run_bass_kernel_spmd as _run

    nc = _bacc.Bacc("TRN2", target_bir_lowering=False, num_devices=1)
    arrays, args = {}, []
    for name in _INS:
        a = _np.ascontiguousarray(inputs[name])
        arrays[f"in_{name}_dram"] = a
        args.append(nc.dram_tensor(f"in_{name}_dram", a.shape, _mybir.dt.from_np(a.dtype), kind="ExternalInput").ap())
    shape = inputs["x"].shape
    res = nc.dram_tensor("out_dram", shape, _mybir.dt.float32, kind="ExternalOutput").ap()
    conv_block_kernel(nc, *args, res)
    r = _run(nc, [arrays], core_ids=[0])
    return r.results[0]["out_dram"]
```

```python
import concourse.bass as bass
from concourse import mybir
from contextlib import ExitStack


class Count:

    def __init__(self, g, a, b):
        self.g, self.a, self.b = g, a, b

    def __add__(self, n):
        return Count(self.g, self.a, self.b + n)

    def __sub__(self, n):
        return Count(self.g, self.a, self.b - n)

    def __mul__(self, n):
        return Count(self.g, self.a * n, self.b * n)

    __radd__, __rmul__ = __add__, __mul__

    def address(self):
        return self.g * self.a + self.b


def address(n):
    return n if isinstance(n, int) else n.address()


def conv_block_kernel(nc, x, offset, w77, b77, w53, b53, w35, b35, w7w, w7h, w5w, w5h, out):
    f32, f16, i32 = mybir.dt.float32, mybir.dt.float16, mybir.dt.int32
    ALU, AX = mybir.AluOpType, mybir.AxisListType
    ACT = mybir.ActivationFunctionType
    IDENT, EXP, SQRT = ACT.Identity, ACT.Exp, ACT.Sqrt

    B, C, H, W = x.shape
    P = 128
    GC = 12
    NG = C // GC
    BC = 4
    NQ = GC // BC
    NH = 2
    PERIOD = NH * NQ
    NI = B // NH // 2
    NP = NI * W
    BLK = BC * NP
    NBLOCKS = NG * PERIOD
    DMAS = 16 * BC * 2
    L0_DMAS = 16 * 3
    LAG = 4
    UNITS = 3
    PC = 8
    NBQ = C // BC
    K = 7
    R = K // 2
    TAPS = 2 * K
    PITCH = H + K - 1
    ROW = TAPS * PITCH
    FIRST = H - 1 - R
    N0STR = 2 * W
    ACT_SCALE = 64.0
    L0_SCALE = 256.0
    EPS = 1e-5
    KTOP = 128.0
    assert PC % BC == 0 and NBQ <= P
    CP = min(P, C)
    CT = C // CP

    x_v = x.rearrange("(h i r) (g q c) y x -> g q c h r y i x", h=NH, r=2, q=NQ, c=BC)
    out_v = out.rearrange("(h i r) (g q c) y x -> g q c h r y i x", h=NH, r=2, q=NQ, c=BC)

    hankel_d = nc.dram_tensor("hankel_scratch", (C * ROW + P,), f16, kind="Internal").ap()
    shift_d = nc.dram_tensor("shift_scratch", (NBQ, 2, 2 * H), f16, kind="Internal").ap()
    l0_coef_d = nc.dram_tensor("l0_coef_scratch", (NBQ, 4), f32, kind="Internal").ap()
    l1_coef_d = nc.dram_tensor("l1_coef_scratch", (C, 4), f32, kind="Internal").ap()

    ctx = ExitStack()
    with ctx:
        def sb(name, shape, dt):
            return ctx.enter_context(nc.sbuf_tensor(name, shape, dt))

        def pb(name, shape):
            return ctx.enter_context(nc.psum_tensor(name, shape, f32))

        def sem(name):
            return ctx.enter_context(nc.semaphore(name))

        X = sb("X", [P, UNITS, NQ, BLK], f32)
        N0 = sb("N0", [P, W + BC * NI * N0STR + W], f32)
        U = sb("U", [P, BLK], f32)
        UH = sb("UH", [P, BLK], f16)
        UL = sb("UL", [P, BLK], f16)
        N1 = sb("N1", [P, BLK], f32)
        H1 = sb("H1", [P, 2, BLK], f16)
        L1 = sb("L1", [P, 2, BLK], f16)
        HK = sb("HK", [P, 2, ROW], f16)
        WT = sb("WT", [P, GC, TAPS, P], f16)
        MY = sb("MY", [P, NQ, 2, P], f16)
        HM = sb("HM", [P, NQ, 2, H], f16)
        C0 = sb("C0", [P, NQ, 4], f32)
        MASK = sb("MASK", [P, 2], f32)
        C1 = sb("C1", [P, NQ, BC, 4], f32)
        PAR = sb("PAR", [P, P], f32)
        BN = [sb("BN0", [P, NI, NQ, 6], f32), sb("BN1", [P, NI, NQ, 6], f32)]
        SQ = [sb("SQ0", [P, NI * NQ * 2], f32), sb("SQ1", [P, NI * NQ * 2], f32)]
        SUMS = [sb("SUMS0", [P, 2 * NI], f32), sb("SUMS1", [P, 2 * NI], f32)]
        MOM = [sb("MOM0", [P, 4 * NI], f32), sb("MOM1", [P, 4 * NI], f32)]
        COEF = [sb("COEF0", [P, NH, 2 * NI], f32), sb("COEF1", [P, NH, 2 * NI], f32)]

        ps_l0 = pb("ps_l0", [P, BC * NP])
        ps_l1 = [pb(f"ps_l1_{n}", [P, NP]) for n in range(3)]
        ps_sum = pb("ps_sum", [P, 2, 2 * NI])

        GT = N1[0:CP, :].bitcast(f16)[:, 0:CT * ROW].rearrange("p (t a m) -> p t a m", t=CT, a=TAPS)
        ZERO = sb("ZERO", [1, P], f16)
        small = {}
        for name, n in (("w77", K * K), ("w53", 15), ("w35", 15), ("w7w", 7), ("w7h", 7), ("w5w", 5),
                        ("w5h", 5), ("b77", 1), ("b53", 1), ("b35", 1)):
            small[name] = sb("in_" + name, [CP, CT, n], f32)
        KK = sb("KK", [CP, CT, K * K], f32)
        KT = sb("KT", [CP, CT, K * K], f32)
        KH = sb("KH", [CP, CT, K * K], f16)
        KM = sb("KM", [CP, CT, 1], f32)
        KI = sb("KI", [CP, CT, 1], f32)
        KS = sb("KS", [CP, CT, 1], f32)
        KC = sb("KC", [CP, CT, 4], f32)
        OFF = sb("OFF", [NBQ, 2], f32)
        RND = sb("RND", [NBQ, 2], f32)
        FRAC = sb("FRAC", [NBQ, 2], f32)
        DSQ = sb("DSQ", [NBQ, 3, 2], f32)
        EX = sb("EX", [NBQ, 3, 2], f32)
        WARM = sb("WARM", [NBQ, 1], f32)
        NRM = sb("NRM", [NBQ, 4], f32)
        TY = sb("TY", [NBQ, 3], f32)
        CC = sb("CC", [NBQ, 4], f32)
        DIFF = sb("DIFF", [NBQ, 2 * H], f32)
        ACC = sb("ACC", [NBQ, 2 * H], f32)
        TMP = sb("TMP", [NBQ, 2 * H], f32)
        MHL = sb("MHL", [NBQ, 2, 2 * H], f16)
        PIDX = sb("PIDX", [P, 1], f32)
        EIDX = sb("EIDX", [P, 2 * H], f32)
        YIDX = sb("YIDX", [P, 1], f32)
        PHALF = sb("PHALF", [P, 1], f32)
        MHALF = sb("MHALF", [P, P], f32)

        x_loaded = [sem(f"x_loaded{n}") for n in range(PERIOD)]
        stored = [sem(f"stored{n}") for n in range(PERIOD)]
        l0_matrix_loaded = [sem(f"l0_matrix_loaded{n}") for n in range(NQ)]
        l1_coef_loaded = [sem(f"l1_coef_loaded{n}") for n in range(NQ)]
        hankel_loaded = [sem(f"hankel_loaded{n}") for n in range(2)]
        small_loaded = sem("small_loaded")
        offset_loaded = sem("offset_loaded")
        index_ready = sem("index_ready")
        pads_ready = sem("pads_ready")
        blocks_ready = sem("blocks_ready")
        prep = sem("prep")
        exps_in = sem("exps_in")
        exps_ready = sem("exps_ready")
        parity_ready = sem("parity_ready")
        shifts_ready = sem("shifts_ready")
        tables_ready = sem("tables_ready")
        prologue_done = sem("prologue_done")
        l0_scratch_stored = sem("l0_scratch_stored")
        l1_scratch_stored = sem("l1_scratch_stored")
        mask_ready = sem("mask_ready")
        l0_matrix_ready = sem("l0_matrix_ready")
        n0_ready = sem("n0_ready")
        taps_part = sem("taps_part")
        u_ready = sem("u_ready")
        uh_ready = sem("uh_ready")
        ul_ready = sem("ul_ready")
        l0_done = sem("l0_done")
        x1_ready = sem("x1_ready")
        bn_done = [sem("bn0_done"), sem("bn1_done")]
        chain = [sem("chain0"), sem("chain1")]
        sums_ready = [sem("sums0_ready"), sem("sums1_ready")]
        sums_done = [sem("sums0_done"), sem("sums1_done")]
        var_ready = [sem("var0_ready"), sem("var1_ready")]
        scale_ready = [sem("scale0_ready"), sem("scale1_ready")]
        coef_ready = [sem("coef0_ready"), sem("coef1_ready")]
        n1_ready = sem("n1_ready")
        h1_ready = sem("h1_ready")
        l1_ready = sem("l1_ready")
        matrix_ready = sem("matrix_ready")
        conv_done = sem("conv_done")
        z_ready = sem("z_ready")
        out_ready = sem("out_ready")

        CHAIN = 6

        def slots(eng, g):
            if isinstance(g, int):
                return [(2 * g + d) % UNITS for d in range(UNITS)]
            return [eng.snap((address(g) * 2 + d) % UNITS) for d in range(UNITS)]

        def xblock(slot, g, k):
            s = slot[(k // NQ) % UNITS]
            return X[:, bass.ds(s, 1), k % NQ, :].rearrange("p a n -> p (a n)")

        def blocks(eng, body, last):
            body(0, range(PERIOD))
            with eng.Fori(0, NG - 2) as g:
                body(Count(g, 1, 1), range(PERIOD))
            body(NG - 1, range(PERIOD + last))

        def live(g, k):
            return not isinstance(g, int) or 0 <= g * PERIOD + k < NBLOCKS

        def counter(eng):
            product = eng.alloc_register(f"product_{eng.engine.name}")
            count = eng.alloc_register(f"count_{eng.engine.name}")

            def nth(value):
                if isinstance(value, int):
                    return value
                eng.reg_mul(product, value.g, value.a)
                eng.reg_add(count, product, value.b)
                eng.wait_ge(prologue_done, 1)
                return count
            return nth

        def unfolded(g, k):
            return [((k - d) // PERIOD, (k - d) % PERIOD * BC + c) for d, c0 in ((3, 2), (2, 0)) for c in (c0, c0 + 1)
                    if live(g, k - d) and (k - d) % PERIOD < NQ]

        block = ctx.enter_context(nc.Block())

        @block.sync
        def _(sp):
            nth = counter(sp)
            sp.dma_start(OFF[:, :], bass.AP(tensor=offset.tensor, offset=0, ap=[[2, C // PC], [0, PC // BC], [1, 2]]))\
                .then_inc(offset_loaded, 16)
            def load_x(g, k):
                dk = k % PERIOD
                gg = g + k // PERIOD
                if live(g, k - UNITS * NQ):
                    old = k - UNITS * NQ
                    sp.wait_ge(stored[old % PERIOD], nth(DMAS * (g + old // PERIOD + 1)))
                dst = xblock(s3, g, k)
                for c in range(BC):
                    for r in range(2):
                        sp.dma_start(dst[r * H:(r + 1) * H, c * NP:(c + 1) * NP].rearrange("p (i x) -> p i x", i=NI),
                                     x_v[bass.ds(address(gg), 1), dk % NQ, c, dk // NQ, r].rearrange("g y i x -> (g y) i x"))\
                            .then_inc(x_loaded[dk], 16)

            def store(g, k):
                dk = k % PERIOD
                gg = g + k // PERIOD
                src = xblock(s3, g, k)
                sp.wait_ge(out_ready, nth((g * PERIOD + k + 1) * BC))
                for c in range(BC):
                    for r in range(2):
                        sp.dma_start(out_v[bass.ds(address(gg), 1), dk % NQ, c, dk // NQ, r].rearrange("g y i x -> (g y) i x"),
                                     src[r * H:(r + 1) * H, c * NP:(c + 1) * NP].rearrange("p (i x) -> p i x", i=NI))\
                            .then_inc(stored[dk], 16)

            def load_l0(g, q):
                if not isinstance(g, int) or g > 0:
                    sp.wait_ge(l0_done, nth(2 * (g * PERIOD - NQ + q + 1)))
                n = g * NQ + q
                for r in range(2):
                    sp.dma_start(HM[r * H:(r + 1) * H, q, :, :],
                                 bass.AP(tensor=shift_d.tensor, offset=address(n * (4 * H)),
                                         ap=[[1, H], [2 * H, 2], [1, H]])).then_inc(l0_matrix_loaded[q], 16)
                sp.dma_start(C0[:, q, :], bass.AP(tensor=l0_coef_d.tensor, offset=address(n * 4), ap=[[0, P], [1, 4]]))\
                    .then_inc(l0_matrix_loaded[q], 16)

            def load_l1_coef(g, q):
                if not isinstance(g, int) or g > 0:
                    sp.wait_ge(out_ready, nth((g * PERIOD - NQ + q + 1) * BC))
                sp.dma_start(C1[:, q, :, :].rearrange("p c k -> p (c k)"),
                             bass.AP(tensor=l1_coef_d.tensor, offset=address((g * NQ + q) * BC * 4),
                                     ap=[[0, P], [1, BC * 4]])).then_inc(l1_coef_loaded[q], 16)

            def load_hankel(g, c):
                n = g * GC + c
                if not isinstance(g, int) or n >= 2:
                    sp.wait_ge(matrix_ready, nth(n - 1))
                sp.dma_start(HK[:, c % 2, :],
                             bass.AP(tensor=hankel_d.tensor, offset=address(n * ROW), ap=[[0, 2], [1, H], [1, ROW]]))\
                    .then_inc(hankel_loaded[c % 2], 16)

            s3 = slots(sp, 0)
            for k in range(3):
                load_x(0, k)
            flat = {"w77": w77, "w53": w53, "w35": w35, "w7w": w7w, "w7h": w7h, "w5w": w5w, "w5h": w5h}
            for name, w in flat.items():
                sp.dma_start(small[name][:, :, :], w.rearrange("(t p) a h w -> p t (a h w)", p=CP))\
                    .then_inc(small_loaded, 16)
            with nc.allow_non_contiguous_dma(reason="a few hundred biases"):
                for name, b in (("b77", b77), ("b53", b53), ("b35", b35)):
                    sp.dma_start(small[name][:, :, :], b.rearrange("(t p k) -> p t k", p=CP, k=1))\
                        .then_inc(small_loaded, 16)
            sp.wait_ge(shifts_ready, 1)
            sp.dma_start(l0_coef_d, CC[:, :]).then_inc(l0_scratch_stored, 16)
            sp.dma_start(shift_d, MHL[:, :, :]).then_inc(l0_scratch_stored, 16)
            sp.wait_ge(l0_scratch_stored, 32)
            for q in range(2):
                load_l0(0, q)
            load_x(0, 3)
            sp.wait_ge(tables_ready, 1)
            sp.dma_start(hankel_d[0:C * ROW].rearrange("(t p n) -> p t n", p=CP, n=ROW),
                         GT[:, :, :, :].rearrange("p t a m -> p t (a m)")).then_inc(l1_scratch_stored, 16)
            sp.dma_start(hankel_d[C * ROW:C * ROW + P].rearrange("(a n) -> a n", a=1), ZERO[:, :])\
                .then_inc(l1_scratch_stored, 16)
            sp.dma_start(l1_coef_d.rearrange("(t p) k -> p t k", p=CP), KC[:, :, :]).then_inc(l1_scratch_stored, 16)
            sp.wait_ge(l1_scratch_stored, 16 * 3)
            for c in range(2):
                load_hankel(0, c)

            def steps(g, ks):
                nonlocal s3
                s3 = slots(sp, g)
                for k in ks:
                    if live(g, k - LAG - 1):
                        store(g, k - LAG - 1)
                    if live(g, k + 2) and (k + 2) % PERIOD < NQ:
                        load_l0(g + (k + 2) // PERIOD, (k + 2) % PERIOD)
                    if live(g, k - 2) and (k - 2) % PERIOD < NQ:
                        load_l1_coef(g + (k - 2) // PERIOD, (k - 2) % PERIOD)
                    for d, c in unfolded(g, k)[2:]:
                        load_hankel(g + d, c)
                    if live(g, k + 4):
                        load_x(g, k + 4)
                    for d, c in unfolded(g, k + 1)[:2]:
                        if isinstance(g, Count) or (g, k) != (0, 1):
                            load_hankel(g + d, c)

            blocks(sp, steps, LAG + 1)
            for n in range(PERIOD):
                sp.wait_ge(stored[n], DMAS * NG)

        @block.gpsimd
        def _(pool):
            nth = counter(pool)
            pool.iota(PIDX[:, :], [[0, 1]], base=0, channel_multiplier=1,
                      allow_small_or_imprecise_dtypes=True).then_inc(index_ready, 1)
            pool.iota(EIDX[:, :], [[1, 2 * H]], base=1 - H, channel_multiplier=0,
                      allow_small_or_imprecise_dtypes=True).then_inc(index_ready, 1)
            pool.memset(N0[:, :], 0.0).then_inc(pads_ready, 1)
            pool.memset(MY[:, :, :, :].bitcast(f32), 0.0).then_inc(blocks_ready, 1)
            pool.memset(WT[:, :, :, :].bitcast(f32), 0.0).then_inc(blocks_ready, 1)

            def steps(g, ks):
                for k in ks:
                    if live(g, k):
                        for n in range(2):
                            half = slice(n * 2 * NP, (n + 1) * 2 * NP)
                            pool.wait_ge(uh_ready, nth(2 * (g * PERIOD + k) + n + 1))
                            if live(g, k - 1):
                                pool.wait_ge(l0_done, nth(2 * (g * PERIOD + k) - 1 + n))
                            pool.tensor_tensor(UL[:, half], U[:, half], UH[:, half], ALU.subtract).then_inc(ul_ready, 1)
                    kb = k - LAG + 1
                    if live(g, kb):
                        pool.wait_ge(h1_ready, nth(g * PERIOD + kb + 1))
                        if live(g, kb - 2):
                            pool.wait_ge(conv_done, nth((g * PERIOD + kb - 1) * BC))
                        pool.tensor_tensor(L1[:, kb % 2, :], N1[:, :],
                                           H1[:, kb % 2, :], ALU.subtract).then_inc(l1_ready, 1)

            blocks(pool, steps, LAG)

        @block.scalar
        def _(act):
            nth = counter(act)
            act.wait_ge(exps_in, 1)
            act.activation(EX[:, :, :], DSQ[:, :, :], EXP, scale=-2.0).then_inc(exps_ready, 1)
            act.wait_ge(exps_ready, 1)
            act.activation(WARM[:, :], EX[:, 0, 0:1], SQRT)
            act.wait_ge(pads_ready, 1)

            def normalise(g, k, kind, dst, done):
                src = xblock(s3, g, k).rearrange("p (c i x) -> p c i x", c=BC, i=NI)
                h = (k // NQ) % NH
                for i in range(NI):
                    ins = act.activation(dst[:, :, i, :], src[:, :, i, :], IDENT,
                                         scale=COEF[kind][:, h, i:i + 1], bias=COEF[kind][:, h, NI + i:NI + i + 1])
                ins.then_inc(done, 1)

            def root(g, k, kind):
                unit, h = g * NH + k // NQ, (k // NQ) % NH
                act.wait_ge(var_ready[kind], nth(unit + 1))
                act.activation(COEF[kind][:, h, 0:NI], MOM[kind][:, 3 * NI:4 * NI], SQRT, scale=ACT_SCALE ** 2)\
                    .then_inc(scale_ready[kind], 1)

            def result(g, k, c):
                act.wait_ge(z_ready, nth((g * PERIOD + k) * BC + c + 1))
                v = xblock(s3, g, k)[:, c * NP:(c + 1) * NP]
                q = k % NQ
                act.activation(v, v, IDENT, scale=C1[:, q, c, 1:2], bias=C1[:, q, c, 2:3]).then_inc(out_ready, 1)

            n0_images = N0[:, W:W + BC * NI * N0STR].rearrange("p (c i x) -> p c i x", c=BC, i=NI)[:, :, :, 0:W]
            n1_images = N1[:, :].rearrange("p (c i x) -> p c i x", c=BC, i=NI)

            def normalise_l0(g, k):
                act.wait_ge(coef_ready[0], nth(g * NH + k // NQ + 1))
                if live(g, k - 1):
                    act.wait_ge(u_ready, nth(2 * (g * PERIOD + k)))
                normalise(g, k, 0, n0_images, n0_ready)

            def steps(g, ks):
                nonlocal s3
                s3 = slots(act, g)
                for k in ks:
                    if live(g, k - LAG - 1):
                        result(g, k - LAG - 1, 3)
                    if live(g, k):
                        for n in range(2):
                            half = slice(n * 2 * NP, (n + 1) * 2 * NP)
                            act.wait_ge(u_ready, nth(2 * (g * PERIOD + k) + n + 1))
                            if live(g, k - 1):
                                act.wait_ge(l0_done, nth(2 * (g * PERIOD + k) - 1 + n))
                            act.activation(UH[:, half], U[:, half], IDENT).then_inc(uh_ready, 1)
                    if live(g, k - 1) and (k - 1) % NQ == NQ - 1:
                        root(g, k - 1, 1)
                    kb = k - LAG + 1
                    if live(g, kb):
                        act.wait_ge(coef_ready[1], nth(g * NH + kb // NQ + 1))
                        if live(g, kb - 1):
                            act.wait_ge(l1_ready, nth(g * PERIOD + kb))
                        normalise(g, kb, 1, n1_images, n1_ready)
                        act.wait_ge(n1_ready, nth(g * PERIOD + kb + 1))
                        if live(g, kb - 2):
                            act.wait_ge(conv_done, nth((g * PERIOD + kb - 1) * BC))
                        act.activation(H1[:, kb % 2, :], N1[:, :], IDENT)\
                            .then_inc(h1_ready, 1)
                    if live(g, k - LAG):
                        result(g, k - LAG, 0)
                        result(g, k - LAG, 1)
                    if live(g, k + 3) and (k + 3) % NQ == NQ - 1:
                        root(g, k + 3, 0)
                    if live(g, k + 1):
                        normalise_l0(g, k + 1)
                    if live(g, k - LAG):
                        result(g, k - LAG, 2)

            s3 = slots(act, 0)
            root(0, 0, 0)
            normalise_l0(0, 0)
            blocks(act, steps, LAG + 1)

        @block.vector
        def _(dve):
            nth = counter(dve)
            count = [0]

            def step(ins):
                count[0] += 1
                ins.then_inc(prep, 1)
                dve.wait_ge(prep, count[0])

            dve.wait_ge(offset_loaded, 16)
            step(dve.tensor_scalar(OFF[:, :], OFF[:, :], -1000.0, 1000.0, ALU.max, ALU.min))
            step(dve.tensor_scalar(RND[:, :], OFF[:, :], 12582912.0, None, ALU.add))
            step(dve.tensor_scalar(RND[:, :], RND[:, :], -12582912.0, None, ALU.add))
            step(dve.tensor_tensor(FRAC[:, :], OFF[:, :], RND[:, :], ALU.subtract))
            for t in range(3):
                step(dve.tensor_scalar(DSQ[:, t, :], FRAC[:, :], float(t - 1), None, ALU.add))
            for t in range(3):
                ins = dve.tensor_tensor(DSQ[:, t, :], DSQ[:, t, :], DSQ[:, t, :], ALU.mult)
            step(ins)
            dve.nop().then_inc(exps_in, 1)
            dve.wait_ge(index_ready, 2)
            step(dve.tensor_scalar(PHALF[:, :], PIDX[:, :], float(H), None, ALU.is_ge))
            step(dve.tensor_scalar(MHALF[:, :], EIDX[:, :], 1.0, None, ALU.is_ge))
            dve.tensor_scalar(PAR[:, :], MHALF[:, :], PHALF[:, 0:1], None, ALU.is_equal).then_inc(parity_ready, 1)
            step(dve.scalar_tensor_tensor(YIDX[:, :], PHALF[:, :], -float(H), PIDX[:, :], ALU.mult, ALU.add))
            dve.wait_ge(exps_ready, 1)
            step(dve.tensor_reduce(NRM[:, 0:2], EX[:, :, :].rearrange("p t k -> p k t"), AX.X, ALU.add))
            step(dve.tensor_tensor(NRM[:, 2:3], NRM[:, 0:1], NRM[:, 1:2], ALU.mult))
            step(dve.reciprocal(NRM[:, 2:3], NRM[:, 2:3]))
            step(dve.scalar_tensor_tensor(NRM[:, 2:3], NRM[:, 2:3], L0_SCALE, EX[:, 1, 0:1], ALU.mult, ALU.mult))
            dve.tensor_scalar(TY[:, :], EX[:, :, 1], NRM[:, 2:3], None, ALU.mult)
            step(dve.reciprocal(NRM[:, 3:4], EX[:, 1, 0:1]))
            dve.tensor_tensor(CC[:, 0:1], EX[:, 0, 0:1], NRM[:, 3:4], ALU.mult)
            dve.tensor_tensor(CC[:, 1:2], EX[:, 2, 0:1], NRM[:, 3:4], ALU.mult)
            step(dve.tensor_scalar(NRM[:, 0:1], RND[:, 0:1], float(-W), float(W), ALU.max, ALU.min))
            step(dve.tensor_scalar(NRM[:, 0:1], NRM[:, 0:1], -1.0, float(W), ALU.mult, ALU.add))
            dve.tensor_copy(CC[:, 2:3].bitcast(i32), NRM[:, 0:1])
            step(dve.tensor_copy(CC[:, 3:4], RND[:, 1:2]))
            step(dve.tensor_scalar(DIFF[:, :], EIDX[0:NBQ, :], CC[:, 3:4], None, ALU.add))
            for t in range(3):
                dst = ACC if t == 0 else TMP
                step(dve.tensor_scalar(dst[:, :], DIFF[:, :], float(t - 1), TY[:, t:t + 1], ALU.is_equal, ALU.mult))
                if t > 0:
                    step(dve.tensor_tensor(ACC[:, :], ACC[:, :], TMP[:, :], ALU.add))
            step(dve.tensor_copy(MHL[:, 0, :], ACC[:, :]))
            dve.tensor_tensor(MHL[:, 1, :], ACC[:, :], MHL[:, 0, :], ALU.subtract).then_inc(shifts_ready, 1)

            def l1_tables():
                dve.wait_ge(small_loaded, 16 * 10)
                dve.memset(ZERO[:, :], 0.0)
                dve.wait_ge(blocks_ready, 2)
                step(dve.memset(GT, 0.0))
                kk = KK[:, :, :].rearrange("p t (i j) -> p t i j", i=K)
                kt = KT[:, :, :].rearrange("p t (i j) -> p t i j", i=K)

                def col(name, n):
                    return small[name][:, :, :].rearrange("p t (i j) -> p t i j", j=1).to_broadcast([CP, CT, n, n])

                def row(name, n):
                    return small[name][:, :, :].rearrange("p t (i j) -> p t i j", i=1).to_broadcast([CP, CT, n, n])
                step(dve.tensor_tensor(kt, col("w7h", 7), row("w7w", 7), ALU.mult))
                step(dve.tensor_tensor(kk, kt, small["w77"][:, :, :].rearrange("p t (i j) -> p t i j", i=K), ALU.add))
                for name, i0, ni, nj in (("w53", 1, 5, 3), ("w35", 2, 3, 5)):
                    j0 = R - nj // 2
                    v = kk[:, :, i0:i0 + ni, j0:j0 + nj]
                    step(dve.tensor_tensor(v, v, small[name][:, :, :].rearrange("p t (i j) -> p t i j", i=ni), ALU.add))
                step(dve.tensor_tensor(kt[:, :, 1:6, 1:6], col("w5h", 5), row("w5w", 5), ALU.mult))
                step(dve.tensor_tensor(kk[:, :, 1:6, 1:6], kk[:, :, 1:6, 1:6], kt[:, :, 1:6, 1:6], ALU.add))
                step(dve.tensor_reduce(KM[:, :, :], KK[:, :, :], AX.X, ALU.max, apply_absolute_value=True))
                step(dve.tensor_scalar(KM[:, :, :], KM[:, :, :], 1e-18, None, ALU.max))
                kmi = KM[:, :, :].bitcast(i32)
                step(dve.tensor_scalar(kmi, kmi, 0x7F800000, None, ALU.bitwise_and))
                step(dve.tensor_scalar(KI[:, :, :], KM[:, :, :], 1.0 / KTOP, None, ALU.mult))
                step(dve.reciprocal(KS[:, :, :], KI[:, :, :]))
                dve.tensor_scalar(KC[:, :, 0:1], KS[:, :, :], ACT_SCALE, None, ALU.mult)
                dve.tensor_scalar(KC[:, :, 1:2], KI[:, :, :], 1.0 / ACT_SCALE, None, ALU.mult)
                step(dve.tensor_tensor(KC[:, :, 2:3], small["b77"][:, :, :], small["b53"][:, :, :], ALU.add))
                step(dve.tensor_tensor(KC[:, :, 2:3], KC[:, :, 2:3], small["b35"][:, :, :], ALU.add))
                dve.memset(KC[:, :, 3:4], 0.0)
                step(dve.tensor_tensor(KK[:, :, :], KK[:, :, :], KS[:, :, :].to_broadcast([CP, CT, K * K]), ALU.mult))
                step(dve.tensor_copy(KH[:, :, :], KK[:, :, :]))
                step(dve.tensor_tensor(KT[:, :, :], KK[:, :, :], KH[:, :, :], ALU.subtract))
                for i in range(K):
                    at = FIRST + i
                    dve.tensor_copy(GT[:, :, 0:K, at], KH[:, :, i * K:(i + 1) * K])
                    ins = dve.tensor_copy(GT[:, :, K:TAPS, at], KT[:, :, i * K:(i + 1) * K])
                ins.then_inc(tables_ready, 1)
                dve.nop().then_inc(prologue_done, 1)

            def statistics(g, k, kind):
                if kind == 0:
                    dve.wait_ge(x_loaded[k % PERIOD], nth(DMAS * (g + k // PERIOD + 1)))
                else:
                    dve.wait_ge(x1_ready, nth(2 * (g * PERIOD + k + 1)))
                src = xblock(s3, g, k).rearrange("p (c i x) -> p c i x", c=BC, i=NI)
                for i in range(NI):
                    ins = dve.bn_stats(BN[kind][:, i, k % NQ, :], src[:, :, i, :])
                ins.then_inc(bn_done[kind], 1)

            def links(unit, kind, n):
                def link(ins):
                    nonlocal n
                    n += 1
                    ins.then_inc(chain[kind], 1)
                    dve.wait_ge(chain[kind], nth(unit * CHAIN + n))
                return link

            def row_sums(g, k, kind):
                unit = g * NH + k // NQ
                link = links(unit, kind, 0)
                cnt = BC * W / 2
                tup = BN[kind][:, :, :, :].rearrange("p i q (e v) -> p (i q e) v", v=3)
                dve.wait_ge(bn_done[kind], nth((unit + 1) * NQ))
                link(dve.scalar_tensor_tensor(SQ[kind][:, :], tup[:, :, 1], cnt, tup[:, :, 1], ALU.mult, ALU.mult))
                link(dve.tensor_tensor(SQ[kind][:, :], SQ[kind][:, :], tup[:, :, 2], ALU.add))
                dve.tensor_reduce(SUMS[kind][:, 0:NI], tup[:, :, 1].rearrange("p (i n) -> p i n", n=2 * NQ),
                                  AX.X, ALU.add)
                dve.tensor_reduce(SUMS[kind][:, NI:2 * NI], SQ[kind][:, :].rearrange("p (i n) -> p i n", n=2 * NQ),
                                  AX.X, ALU.add).then_inc(sums_ready[kind], 1)

            def variances(g, k, kind):
                unit = g * NH + k // NQ
                link = links(unit, kind, 2)
                mean, sq, var, rs = (MOM[kind][:, j * NI:(j + 1) * NI] for j in range(4))
                dve.wait_ge(sums_done[kind], nth(unit + 1))
                link(dve.tensor_scalar(mean, ps_sum[:, kind, 0:NI], 1.0 / (H * 2 * NQ), None, ALU.mult))
                link(dve.tensor_tensor(sq, mean, mean, ALU.mult))
                link(dve.scalar_tensor_tensor(var, ps_sum[:, kind, NI:2 * NI], 1.0 / (GC * H * W), sq,
                                              ALU.mult, ALU.subtract))
                link(dve.tensor_scalar(rs, var, 0.0, EPS, ALU.max, ALU.add))
                dve.reciprocal(rs, rs).then_inc(var_ready[kind], 1)

            def shifts(g, k, kind):
                unit = g * NH + k // NQ
                h = (k // NQ) % NH
                mean, scale, shift = MOM[kind][:, 0:NI], COEF[kind][:, h, 0:NI], COEF[kind][:, h, NI:2 * NI]
                dve.wait_ge(scale_ready[kind], nth(unit + 1))
                dve.scalar_tensor_tensor(shift, mean, -1.0, scale, ALU.mult, ALU.mult)\
                    .then_inc(coef_ready[kind], 1)

            def unfold(g, c):
                n = g * GC + c
                dve.wait_ge(hankel_loaded[c % 2], nth(16 * (g * (GC // 2) + c // 2 + 1)))
                if not isinstance(g, int) or g > 0:
                    dve.wait_ge(conv_done, nth((g * PERIOD - NQ) * BC + c + 1))
                for r in range(2):
                    own = slice(r * H, (r + 1) * H)
                    ins = dve.tensor_copy(WT[own, c, :, own],
                                          HK[own, c % 2, :].rearrange("p (a m) -> p a m", a=TAPS)[:, :, H - 1::-1])
                ins.then_inc(matrix_ready, 1)

            def l0_matrix(g, q):
                n = g * NQ + q
                dve.wait_ge(l0_matrix_loaded[q], nth(L0_DMAS * (g + 1)))
                if not isinstance(g, int) or g > 0:
                    dve.wait_ge(l0_done, nth(2 * (g * PERIOD - NQ + q + 1)))
                dve.tensor_scalar(MASK[:, 0:1], YIDX[:, :], C0[:, q, 3:4], 0.0, ALU.add, ALU.is_ge)
                dve.tensor_scalar(MASK[:, 1:2], YIDX[:, :], C0[:, q, 3:4], float(H - 1), ALU.add, ALU.is_le)\
                    .then_inc(mask_ready, 1)
                dve.wait_ge(mask_ready, nth(n + 1))
                for r in range(2):
                    own = slice(r * H, (r + 1) * H)
                    ins = dve.tensor_scalar(MY[own, q, :, own], HM[own, q, :, H - 1::-1], MASK[own, 0:1], MASK[own, 1:2],
                                            ALU.mult, ALU.mult)
                ins.then_inc(l0_matrix_ready, 1)

            def taps_x(g, k):
                q = k % NQ
                dve.wait_ge(l0_matrix_loaded[q], nth(L0_DMAS * (g + 1)))
                at = dve.value_load(C0[0:1, q, 2:3].bitcast(i32), min_val=0, max_val=2 * W)
                dve.wait_ge(n0_ready, nth(g * PERIOD + k + 1))
                for n in range(2):
                    if live(g, k - 1):
                        dve.wait_ge(ul_ready, nth(2 * (g * PERIOD + k) - 1 + n))
                    v = N0[:, bass.ds(at + n * (BC // 2 * NI * N0STR), BC // 2 * NI * N0STR)]\
                        .rearrange("p (n x) -> p n x", x=N0STR)
                    u = U[:, n * 2 * NP:(n + 1) * 2 * NP].rearrange("p (n x) -> p n x", x=W)
                    dve.tensor_copy(u[:, :, 0:1], v[:, :, 0:1])
                    dve.scalar_tensor_tensor(u[:, :, 1:W], v[:, :, 0:W - 1], C0[:, q, 0:1], v[:, :, 1:W],
                                             ALU.mult, ALU.add).then_inc(taps_part, 1)
                    dve.wait_ge(taps_part, nth(2 * (g * PERIOD + k) + n + 1))
                    dve.scalar_tensor_tensor(u[:, :, 0:W - 1], v[:, :, 1:W], C0[:, q, 1:2], u[:, :, 0:W - 1],
                                             ALU.mult, ALU.add).then_inc(u_ready, 1)

            def ahead(g, k):
                return isinstance(g, int) and 1 <= g * PERIOD + k < NQ

            def evacuate(g, k):
                dst = xblock(s3, g, k)
                for n in range(2):
                    dve.wait_ge(l0_done, nth(2 * (g * PERIOD + k) + n + 1))
                    v = dst[:, n * 2 * NP:(n + 1) * 2 * NP]
                    dve.scalar_tensor_tensor(v, ps_l0[:, n * 2 * NP:(n + 1) * 2 * NP], 1.0 / (ACT_SCALE * L0_SCALE),
                                             v, ALU.mult, ALU.add).then_inc(x1_ready, 1)

            def residual(g, k, c):
                q = k % NQ
                if c == 0:
                    dve.wait_ge(l1_coef_loaded[q], nth(16 * (g + k // PERIOD + 1)))
                dve.wait_ge(conv_done, nth((g * PERIOD + k) * BC + c + 1))
                v = xblock(s3, g, k)[:, c * NP:(c + 1) * NP]
                dve.scalar_tensor_tensor(v, v, C1[:, q, c, 0:1], ps_l1[(k + c) % 3][:, :], ALU.mult, ALU.add)\
                    .then_inc(z_ready, 1)

            def steps(g, ks):
                nonlocal s3
                s3 = slots(dve, g)
                for k in ks:
                    old, new = k - LAG - 1, k - LAG
                    matrices = unfolded(g, k)
                    early = len(matrices) - 2
                    ends1 = live(g, k - 1) and (k - 1) % NQ == NQ - 1
                    ends0 = live(g, k + 3) and (k + 3) % NQ == NQ - 1
                    if live(g, old):
                        residual(g, old, 3)
                    if live(g, k) and not ahead(g, k):
                        taps_x(g, k)
                    if ends1:
                        variances(g, k - 1, 1)
                    if live(g, k) and not ahead(g, k) and k % PERIOD < NQ:
                        l0_matrix(g, k % NQ)
                    if isinstance(g, int) and g + k == 0:
                        l1_tables()
                    if ends1:
                        shifts(g, k - 1, 1)
                    if live(g, new):
                        residual(g, new, 0)
                    if live(g, k + 3):
                        statistics(g, k + 3, 0)
                        if ends0:
                            row_sums(g, k + 3, 0)
                    for d, c in matrices[0:early]:
                        unfold(g + d, c)
                    if live(g, new):
                        residual(g, new, 1)
                    if ends0:
                        variances(g, k + 3, 0)
                    if live(g, new):
                        residual(g, new, 2)
                    if ends0:
                        shifts(g, k + 3, 0)
                    if ahead(g, k + 1):
                        taps_x(g, k + 1)
                        l0_matrix(g, k + 1)
                    if live(g, k):
                        evacuate(g, k)
                        statistics(g, k, 1)
                        if k % NQ == NQ - 1:
                            row_sums(g, k, 1)
                    for d, c in matrices[max(early, 0):]:
                        unfold(g + d, c)

            dve.wait_ge(blocks_ready, 1)
            s3 = slots(dve, 0)
            for k in range(3):
                statistics(0, k, 0)
            row_sums(0, NQ - 1, 0)
            variances(0, NQ - 1, 0)
            shifts(0, NQ - 1, 0)
            blocks(dve, steps, LAG + 1)

        @block.tensor
        def _(pe):
            nth = counter(pe)
            pe.wait_ge(parity_ready, 1)

            def sums(g, k, kind):
                pe.wait_ge(sums_ready[kind], nth(g * NH + k // NQ + 1))
                pe.matmul(ps_sum[:, kind, :], PAR[:, :], SUMS[kind][:, :], start=True, stop=True)\
                    .then_inc(sums_done[kind], 1)

            def l0(g, k):
                q = k % NQ
                pe.wait_ge(l0_matrix_ready, nth(g * NQ + (q + 1 if k < NQ else NQ)))
                for n in range(2):
                    pe.wait_ge(uh_ready, nth(2 * (g * PERIOD + k) + n + 1))
                    pe.wait_ge(ul_ready, nth(2 * (g * PERIOD + k) + n + 1))
                    if live(g, k - 1):
                        pe.wait_ge(x1_ready, nth(2 * (g * PERIOD + k) - 1 + n))
                    for c in (2 * n, 2 * n + 1):
                        cols = slice(c * NP, (c + 1) * NP)
                        for j, (m, v) in enumerate(((0, UH), (0, UL), (1, UH))):
                            ins = pe.matmul(ps_l0[:, cols], MY[:, q, m, :], v[:, cols], start=(j == 0), stop=(j == 2))
                    ins.then_inc(l0_done, 1)

            def l1(g, k, c, parts=range(3)):
                gg, q = g + k // PERIOD, k % NQ
                ch = q * BC + c
                n = (g * PERIOD + k) * BC + c
                if 0 in parts:
                    if c == 0:
                        pe.wait_ge(h1_ready, nth(g * PERIOD + k + 1))
                    pe.wait_ge(matrix_ready, nth(gg * GC + ch + 1))
                    if not isinstance(n, int) or n >= 3:
                        pe.wait_ge(z_ready, nth(n - 2))
                if 2 in parts and c == 0:
                    pe.wait_ge(l1_ready, nth(g * PERIOD + k + 1))
                ps = ps_l1[(k + c) % 3][:, :].rearrange("p (i x) -> p i x", i=NI)
                last = 3 * K - 1
                for t in range(parts[0] * K, (parts[-1] + 1) * K):
                    part = t // K
                    j = (R, *(n for n in range(K) if n != R))[t % K]
                    x0, x1 = max(0, R - j), min(W, W + R - j)
                    src = (H1, H1, L1)[part]
                    low = K if part == 1 else 0
                    v = src[:, k % 2, c * NP:(c + 1) * NP].rearrange("p (i x) -> p i x", i=NI)
                    ins = pe.matmul(ps[:, :, x0:x1], WT[:, ch, low + j, :], v[:, :, x0 + j - R:x1 + j - R],
                                    start=(t == 0), stop=(t == last))
                if parts[-1] == 2:
                    ins.then_inc(conv_done, 1)

            def steps(g, ks):
                for k in ks:
                    old = k - LAG
                    if live(g, old):
                        l1(g, old, 0, (0, 1))
                    if live(g, k - 1) and (k - 1) % NQ == NQ - 1:
                        sums(g, k - 1, 1)
                    if live(g, old):
                        l1(g, old, 0, (2,))
                        l1(g, old, 1)
                        l1(g, old, 2)
                    if live(g, k + 3) and (k + 3) % NQ == NQ - 1:
                        sums(g, k + 3, 0)
                    if live(g, k):
                        l0(g, k)
                    if live(g, old):
                        l1(g, old, 3)

            sums(0, NQ - 1, 0)
            blocks(pe, steps, LAG)


_INS = ["x", "L0_conv_offset", "L1_conv_w77", "L1_conv_b77", "L1_conv_w53", "L1_conv_b53", "L1_conv_w35",
        "L1_conv_b35", "L1_conv_w7w", "L1_conv_w7h", "L1_conv_w5w", "L1_conv_w5h"]


def kernel(**inputs):
    import numpy as _np
    import concourse.bacc as _bacc
    from concourse import mybir as _mybir
    from concourse.bass_utils import run_bass_kernel_spmd as _run

    nc = _bacc.Bacc("TRN2", target_bir_lowering=False, num_devices=1)
    arrays, args = {}, []
    for name in _INS:
        a = _np.ascontiguousarray(inputs[name])
        arrays[f"in_{name}_dram"] = a
        args.append(nc.dram_tensor(f"in_{name}_dram", a.shape, _mybir.dt.from_np(a.dtype), kind="ExternalInput").ap())
    shape = inputs["x"].shape
    res = nc.dram_tensor("out_dram", shape, _mybir.dt.float32, kind="ExternalOutput").ap()
    conv_block_kernel(nc, *args, res)
    r = _run(nc, [arrays], core_ids=[0])
    return r.results[0]["out_dram"]
```
